# Optimizing a Trainium2 kernel written in Bass

```python
import numpy as np
import jax
import jax.numpy as jnp

def _softmax(x, axis=-1):
    return jax.nn.softmax(x, axis=axis)

def _gelu(x):
    return jax.nn.gelu(x, approximate=True)

def _silu(x):
    return jax.nn.silu(x)

def _sigmoid(x):
    return jax.nn.sigmoid(x)

def _layernorm(x, axis=-1, eps=1e-05):
    m = jnp.mean(x, axis=axis, keepdims=True)
    v = jnp.var(x, axis=axis, keepdims=True)
    return (x - m) / jnp.sqrt(v + eps)

def _scatter_add(tgt, idx, src, axis=0):
    return tgt.at[idx].add(src)

def _segment_sum(src, seg, n):
    return jax.ops.segment_sum(src, seg, n)
kernel_name = 'mk_audio_tower_d1_tok_aud1d1024_r4_87796f'

def setup_inputs(seed: int=0):
    np.random.seed(seed)
    _w = jnp.asarray

    def _rec_inputs():
        import jax
        import jax.numpy as jnp
        _rk = jax.random.key(seed)
        x = -0.000296005 + 1.00001 * jax.random.normal(jax.random.fold_in(_rk, 1), (8, 120000), jnp.float32)
        return x
    x = _rec_inputs()

    def _L0_tok_setup():
        import jax, jax.numpy as jnp
        import numpy as np
        RF = 80
        HID = 256
        LN_EPS = 1e-05
        key = jax.random.key(seed)
        k1, k2, k3, k4, k5 = jax.random.split(key, 5)
        waveform = jax.random.normal(k1, (16, 327680), dtype=jnp.float32)
        bound = 1.0 / np.sqrt(RF)
        W = jax.random.uniform(k2, (HID, RF), dtype=jnp.float32, minval=-bound, maxval=bound)
        b = jax.random.uniform(k3, (HID,), dtype=jnp.float32, minval=-bound, maxval=bound)
        ln_gamma = jnp.ones((HID,), dtype=jnp.float32)
        ln_beta = jnp.zeros((HID,), dtype=jnp.float32)
        return {'waveform': waveform, 'W': W, 'b': b, 'ln_gamma': ln_gamma, 'ln_beta': ln_beta}
    _L0_tok_all = _L0_tok_setup()
    _L0_tok_in = {k: v for k, v in _L0_tok_all.items() if k in ('W', 'b', 'ln_gamma', 'ln_beta')}
    del _L0_tok_all

    def _L0_attn_setup():
        import jax, jax.numpy as jnp
        import numpy as np
        HEAD_NUM = 16
        key = jax.random.key(seed)
        ks = jax.random.split(key, 9)
        B, S, D = (4, 512, 256)

        def xavier(k, shape):
            limit = jnp.sqrt(6.0 / (shape[0] + shape[1]))
            return jax.random.uniform(k, shape, jnp.float32, -limit, limit)
        return {'x': jax.random.normal(ks[0], (B, S, D), jnp.float32), 'Wq': xavier(ks[1], (D, D)), 'bq': jnp.zeros((D,), jnp.float32), 'Wk': xavier(ks[2], (D, D)), 'bk': jnp.zeros((D,), jnp.float32), 'Wv': xavier(ks[3], (D, D)), 'bv': jnp.zeros((D,), jnp.float32), 'Wo': xavier(ks[4], (D, D)), 'bo': jnp.zeros((D,), jnp.float32)}
    _L0_attn_all = _L0_attn_setup()
    _L0_attn_in = {k: v for k, v in _L0_attn_all.items() if k in ('Wq', 'bq', 'Wk', 'bk', 'Wv', 'bv', 'Wo', 'bo')}
    del _L0_attn_all

    def _L0_ffn_setup():
        import jax, jax.numpy as jnp
        import numpy as np
        S, B, D, H, DH = (1024, 8, 256, 16, 64)

        def _forward(x, Wg, Wq, bq, Wkv, bkv, Wo, bo, ln_g, ln_b):
            s_len, bsz, d_model = x.shape
            n_head, _, d_head = Wq.shape
            cap = s_len // n_head
            scale = 1.0 / d_head ** 0.5
            h = jnp.transpose(x, (1, 0, 2))
            t = h
            probs = jax.nn.softmax(h @ Wg, axis=-1)
            scores = jnp.transpose(probs, (0, 2, 1))
            _, idx = jax.lax.top_k(scores, cap)
            idx = jnp.sort(idx, axis=-1)
            hg = jnp.take_along_axis(h[:, None, :, :], idx[..., None], axis=2)
            hg = jnp.transpose(hg, (1, 0, 2, 3))
            q = jnp.einsum('hbcd,hde->hbce', hg, Wq) + bq[:, None, None, :]
            kv = jnp.einsum('hbcd,hde->hbce', hg, Wkv) + bkv[:, None, None, :]
            k, v = jnp.split(kv, 2, axis=-1)
            att = jnp.einsum('hbid,hbjd->hbij', q, k) * scale
            p = jax.nn.softmax(att, axis=1)
            av = jnp.einsum('hbij,hbjd->hbid', p, v)
            ao = jnp.einsum('hbid,hde->hbie', av, Wo) + bo
            tok = jnp.transpose(idx, (1, 0, 2))
            b_ids = jnp.arange(bsz)[None, :, None]
            outs = jnp.zeros_like(t).at[b_ids, tok].add(ao)
            y = t + outs
            mu = jnp.mean(y, axis=-1, keepdims=True)
            var = jnp.var(y, axis=-1, keepdims=True)
            yn = (y - mu) * jax.lax.rsqrt(var + 1e-05) * ln_g + ln_b
            return jnp.transpose(yn, (1, 0, 2))
        key = jax.random.key(seed)
        ks = jax.random.split(key, 6)
        s = 0.02
        return {'x': jax.random.normal(ks[0], (S, B, D), jnp.float32), 'attn_mask': jnp.zeros((S, S), jnp.bool_), 'Wg': jax.random.normal(ks[1], (D, H), jnp.float32) * s, 'Wq': jax.random.normal(ks[2], (H, D, DH), jnp.float32) * s, 'bq': jnp.zeros((H, DH), jnp.float32), 'Wkv': jax.random.normal(ks[3], (H, D, 2 * DH), jnp.float32) * s, 'bkv': jnp.zeros((H, 2 * DH), jnp.float32), 'Wo': jax.random.normal(ks[4], (H, DH, D), jnp.float32) * s, 'bo': jnp.zeros((D,), jnp.float32), 'ln_g': jnp.ones((D,), jnp.float32), 'ln_b': jnp.zeros((D,), jnp.float32)}
    _L0_ffn_all = _L0_ffn_setup()
    _L0_ffn_in = {k: v for k, v in _L0_ffn_all.items() if k in ('attn_mask', 'Wg', 'Wq', 'bq', 'Wkv', 'bkv', 'Wo', 'bo', 'ln_g', 'ln_b')}
    del _L0_ffn_all
    return {'x': x, 'L0_tok_W': _L0_tok_in['W'], 'L0_tok_b': _L0_tok_in['b'], 'L0_tok_ln_gamma': _L0_tok_in['ln_gamma'], 'L0_tok_ln_beta': _L0_tok_in['ln_beta'], 'L0_attn_Wq': _L0_attn_in['Wq'], 'L0_attn_bq': _L0_attn_in['bq'], 'L0_attn_Wk': _L0_attn_in['Wk'], 'L0_attn_bk': _L0_attn_in['bk'], 'L0_attn_Wv': _L0_attn_in['Wv'], 'L0_attn_bv': _L0_attn_in['bv'], 'L0_attn_Wo': _L0_attn_in['Wo'], 'L0_attn_bo': _L0_attn_in['bo'], 'L0_ffn_attn_mask': _L0_ffn_in['attn_mask'], 'L0_ffn_Wg': _L0_ffn_in['Wg'], 'L0_ffn_Wq': _L0_ffn_in['Wq'], 'L0_ffn_bq': _L0_ffn_in['bq'], 'L0_ffn_Wkv': _L0_ffn_in['Wkv'], 'L0_ffn_bkv': _L0_ffn_in['bkv'], 'L0_ffn_Wo': _L0_ffn_in['Wo'], 'L0_ffn_bo': _L0_ffn_in['bo'], 'L0_ffn_ln_g': _L0_ffn_in['ln_g'], 'L0_ffn_ln_b': _L0_ffn_in['ln_b']}

def reference(x, L0_tok_W, L0_tok_b, L0_tok_ln_gamma, L0_tok_ln_beta, L0_attn_Wq, L0_attn_bq, L0_attn_Wk, L0_attn_bk, L0_attn_Wv, L0_attn_bv, L0_attn_Wo, L0_attn_bo, L0_ffn_attn_mask, L0_ffn_Wg, L0_ffn_Wq, L0_ffn_bq, L0_ffn_Wkv, L0_ffn_bkv, L0_ffn_Wo, L0_ffn_bo, L0_ffn_ln_g, L0_ffn_ln_b):
    import jax
    import jax.numpy as jnp

    def _L0_tok_ref(waveform, W, b, ln_gamma, ln_beta):
        import jax, jax.numpy as jnp
        import numpy as np
        RF = 80
        HID = 256
        LN_EPS = 1e-05
        B, T = waveform.shape
        x = waveform.reshape(B, T // RF, RF)
        h = jnp.einsum('bfr,hr->bfh', x, W) + b
        mu = jnp.mean(h, axis=-1, keepdims=True)
        var = jnp.mean(jnp.square(h - mu), axis=-1, keepdims=True)
        h = (h - mu) * jax.lax.rsqrt(var + LN_EPS) * ln_gamma + ln_beta
        return h * 0.5 * (1.0 + jax.lax.erf(h / jnp.sqrt(jnp.float32(2.0))))

    def _L0_attn_ref(x, Wq, bq, Wk, bk, Wv, bv, Wo, bo):
        import jax, jax.numpy as jnp
        import numpy as np
        HEAD_NUM = 16
        B, S, D = x.shape
        H = HEAD_NUM
        hd = D // H

        def proj(W, b):
            return (x @ W.T + b).reshape(B, S, H, hd).transpose(0, 2, 1, 3)
        Q, K, V = (proj(Wq, bq), proj(Wk, bk), proj(Wv, bv))
        scale = 1.0 / jnp.sqrt(jnp.float32(hd))
        scores = jnp.einsum('bhqd,bhkd->bhqk', Q, K) * scale
        attn = jax.nn.softmax(scores, axis=-1)
        out = jnp.einsum('bhqk,bhkd->bhqd', attn, V)
        out = out.transpose(0, 2, 1, 3).reshape(B, S, D)
        return out @ Wo.T + bo

    def _L0_ffn_ref(x, attn_mask, Wg, Wq, bq, Wkv, bkv, Wo, bo, ln_g, ln_b):
        import jax, jax.numpy as jnp
        import numpy as np
        S, B, D, H, DH = (1024, 8, 256, 16, 64)

        def _forward(x, Wg, Wq, bq, Wkv, bkv, Wo, bo, ln_g, ln_b):
            s_len, bsz, d_model = x.shape
            n_head, _, d_head = Wq.shape
            cap = s_len // n_head
            scale = 1.0 / d_head ** 0.5
            h = jnp.transpose(x, (1, 0, 2))
            t = h
            probs = jax.nn.softmax(h @ Wg, axis=-1)
            scores = jnp.transpose(probs, (0, 2, 1))
            _, idx = jax.lax.top_k(scores, cap)
            idx = jnp.sort(idx, axis=-1)
            hg = jnp.take_along_axis(h[:, None, :, :], idx[..., None], axis=2)
            hg = jnp.transpose(hg, (1, 0, 2, 3))
            q = jnp.einsum('hbcd,hde->hbce', hg, Wq) + bq[:, None, None, :]
            kv = jnp.einsum('hbcd,hde->hbce', hg, Wkv) + bkv[:, None, None, :]
            k, v = jnp.split(kv, 2, axis=-1)
            att = jnp.einsum('hbid,hbjd->hbij', q, k) * scale
            p = jax.nn.softmax(att, axis=1)
            av = jnp.einsum('hbij,hbjd->hbid', p, v)
            ao = jnp.einsum('hbid,hde->hbie', av, Wo) + bo
            tok = jnp.transpose(idx, (1, 0, 2))
            b_ids = jnp.arange(bsz)[None, :, None]
            outs = jnp.zeros_like(t).at[b_ids, tok].add(ao)
            y = t + outs
            mu = jnp.mean(y, axis=-1, keepdims=True)
            var = jnp.var(y, axis=-1, keepdims=True)
            yn = (y - mu) * jax.lax.rsqrt(var + 1e-05) * ln_g + ln_b
            return jnp.transpose(yn, (1, 0, 2))
        return _forward(x, Wg, Wq, bq, Wkv, bkv, Wo, bo, ln_g, ln_b)
    h = _L0_tok_ref(x, L0_tok_W, L0_tok_b, L0_tok_ln_gamma, L0_tok_ln_beta)
    h = h + _L0_attn_ref(_layernorm(h, axis=-1), L0_attn_Wq, L0_attn_bq, L0_attn_Wk, L0_attn_bk, L0_attn_Wv, L0_attn_bv, L0_attn_Wo, L0_attn_bo)
    h = h + _L0_ffn_ref(_layernorm(h, axis=-1), L0_ffn_attn_mask, L0_ffn_Wg, L0_ffn_Wq, L0_ffn_bq, L0_ffn_Wkv, L0_ffn_bkv, L0_ffn_Wo, L0_ffn_bo, L0_ffn_ln_g, L0_ffn_ln_b)
    return h

_drawn_inputs = setup_inputs


def setup_inputs(seed=0):
    import zlib

    import numpy as np

    out = dict(_drawn_inputs(seed))
    spreads = {'L0_tok_ln_gamma': (1.0, 0.2),
     'L0_tok_ln_beta': (0.0, 0.1),
     'L0_attn_bq': (0.0, 0.448),
     'L0_attn_bk': (0.0, 0.8),
     'L0_attn_bv': (0.0, 0.1),
     'L0_attn_bo': (0.0, 0.1),
     'L0_ffn_bq': (0.0, 0.1),
     'L0_ffn_bkv': (0.0, 0.1),
     'L0_ffn_bo': (0.0, 0.1),
     'L0_ffn_ln_g': (1.0, 0.2),
     'L0_ffn_ln_b': (0.0, 0.1)}
    factors = {}
    for name, (base, spread) in spreads.items():
        noise = np.random.default_rng([zlib.crc32(name.encode()), seed]).standard_normal(out[name].shape)
        drawn = base * np.exp(spread * noise) if base else spread * noise
        out[name] = jnp.asarray(drawn.astype(out[name].dtype))
    for name, factor in factors.items():
        out[name] = (out[name] * factor).astype(out[name].dtype)
    return out
```

```python
import concourse.bass as bass
from concourse import mybir
from contextlib import ExitStack


def audio_tower(nc, x, tok_wT, tok_b, tok_g, tok_be, wqT, bq, wkT, bk, wvT, bv, woT, bo, ln_g, ln_b, out):
    f32, bf16 = mybir.dt.float32, mybir.dt.bfloat16
    ALU, ACT, AX = mybir.AluOpType, mybir.ActivationFunctionType, mybir.AxisListType

    B = x.shape[0]
    RF, D = tok_wT.shape
    S = x.shape[1] // RF
    H = 16
    HD = D // H
    T = 125
    NT = S // T
    QC = 500
    NC = S // QC
    HG = 4
    NG = H // HG
    NCH = NG * NC
    KC = D // 128
    EPS = 1e-5
    SCALE = float(HD) ** -0.5
    assert T * NT == S and QC * NC == S and NCH == NT

    K_PARTS = [0, 1, 2, 0, 1, 0, 2]
    Q_PARTS = [0, 0, 0, 1, 1, 2, 1]
    TERMS = len(K_PARTS)
    MROW = TERMS * HD
    KROWS = MROW + 3

    PGRP = 4
    RING = 3
    PROBS = 6
    SLOTS = 2 * NT
    PV_AHEAD = PROBS // 2

    ERF_P = 0.3275911
    ERF_A = [0.254829592, -0.284496736, 1.421413741, -1.453152027, 1.061405429]
    RSQRT2 = 0.5 ** 0.5

    h_s = nc.dram_tensor("h_scratch", [B, NT, T, D], f32, kind="Internal").ap()
    part_s = nc.dram_tensor("qk_parts_scratch", [B, 3, 2 * D, S], bf16, kind="Internal").ap()
    max_s = nc.dram_tensor("minus_max_scratch", [B, 3, H, S], bf16, kind="Internal").ap()
    o_s = nc.dram_tensor("attended_scratch", [B, D, S], f32, kind="Internal").ap()
    x_v = x.rearrange("b (p u r) -> b p u r", u=NT, r=RF)
    out_v = out.rearrange("b (p u) d -> b p u d", u=NT)

    with ExitStack() as ctx:
        def sb(name, shape, dt=f32):
            return ctx.enter_context(nc.sbuf_tensor(name, shape, dt))

        def sem(name):
            return ctx.enter_context(nc.semaphore(name))

        ident = sb("ident", [128, 128])
        w_tok = sb("w_tok", [RF + 1, D])
        w_qk = sb("w_qk", [128, KC, 2, D])
        w_v = sb("w_v", [128, KC, D])
        w_o = sb("w_o", [128, KC, D])
        b_qk = sb("b_qk", [128, 2 * KC])
        g_tok, be_tok, b_v, b_o, g_ln, be_ln = (sb(n, [T, D]) for n in
                                                ("g_tok", "be_tok", "b_v", "b_o", "g_ln", "be_ln"))
        mhalf = sb("mhalf", [128, 1])
        eps = sb("eps", [128, 1])
        xs = sb("xs", [T, PGRP, RF])
        xT = sb("xT", [RF + 1, PGRP, T])
        hp = sb("hp", [T, PGRP, D])
        ab = sb("ab", [T, PGRP, D])
        ex = sb("ex", [T, PGRP, D])
        tt = sb("tt", [T, PGRP, D])
        qq = sb("qq", [T, PGRP, D])
        hh = sb("hh", [T, PGRP, D])
        zT = sb("zT", [128, PGRP, KC, T])
        fq = sb("fq", [128, PGRP, 2 * KC, T])
        parts = sb("parts", [128, PGRP, 3, 2 * KC, T], bf16)
        stat = sb("stat", [T, PGRP, 6])
        mv = sb("mv", [T, PGRP, 2])
        rs = sb("rs", [T, PGRP, 1])
        stat2 = sb("stat2", [T, PGRP, 6])
        mv2 = sb("mv2", [T, PGRP, 2])
        rs2 = sb("rs2", [T, PGRP, 1])
        QA = sb("QA", [KROWS, 2, HG, S], bf16)
        KA = sb("KA", [KROWS, 2, HG, S], bf16)
        Vb = sb("Vb", [T, 2, NT, D])
        Vst = sb("Vst", [T, NT, HG, 2 * HD])
        prob = sb("prob", [T, PROBS, 2, QC])
        Osb = sb("Osb", [128, QC])
        Den = sb("Den", [128, QC])
        On = sb("On", [128, QC])
        mx = sb("mx", [T, HG * NT])
        mf = sb("mf", [HG * NT, T])
        mparts = sb("mparts", [HG * NT, 3, T], bf16)
        oT = sb("oT", [128, KC, T])
        hE = sb("hE", [T, D])
        s1 = sb("s1", [T, D])
        y1 = sb("y1", [T, D])
        y2 = sb("y2", [T, D])
        estat = sb("estat", [T, 6])
        emv = sb("emv", [T, 2])
        ers = sb("ers", [T, 1])

        PS = ctx.enter_context(nc.psum_tensor("PS", [128, 8, 512], f32))
        PVB, MISC = 6, 7

        s_w, s_id, s_seen, s_ones = sem("s_w"), sem("s_id"), sem("s_seen"), sem("s_ones")
        s_x, s_xT, s_xTs, s_tok, s_var, s_rs = (sem(n) for n in ("s_x", "s_xT", "s_xTs", "s_tok", "s_var", "s_rs"))
        s_nrm, s_hp, s_ex, s_h, s_hst, s_var2, s_rs2 = (sem(n) for n in (
            "s_nrm", "s_hp", "s_ex", "s_h", "s_hst", "s_var2", "s_rs2"))
        s_z, s_zT, s_zTs, s_qk, s_f, s_parts, s_pst, s_v, s_vb = (sem(n) for n in (
            "s_z", "s_zT", "s_zTs", "s_qk", "s_f", "s_parts", "s_pst", "s_v", "s_vb"))
        s_ldm, s_ms, s_mx, s_mt, s_mtT, s_mc, s_cst = (sem(n) for n in (
            "s_ldm", "s_ms", "s_mx", "s_mt", "s_mtT", "s_mc", "s_cst"))
        s_lda, s_sc, s_pr, s_pv, s_vst, s_ov, s_dn, s_on, s_os = (sem(n) for n in (
            "s_lda", "s_sc", "s_pr", "s_pv", "s_vst", "s_ov", "s_dn", "s_on", "s_os"))
        s_el, s_eo, s_s1, s_ev, s_er, s_y2, s_or, s_ost = (sem(n) for n in (
            "s_el", "s_eo", "s_s1", "s_ev", "s_er", "s_y2", "s_or", "s_ost"))
        block = ctx.enter_context(nc.Block())

        def wait(eng, sem_, value):
            eng.wait_ge(sem_, value)
            eng.sem_inc(s_seen, 1)

        WLOADS = 1 + 1 + KC * 4 + 2 * KC + 6

        @block.sync
        def _(sp):
            sp.dma_start(w_tok[0:RF, :], tok_wT).then_inc(s_w, 16)
            sp.dma_start(w_tok[RF:RF + 1, :], tok_b.unsqueeze(0)).then_inc(s_w, 16)
            for c in range(KC):
                rows = slice(c * 128, (c + 1) * 128)
                sp.dma_start(w_qk[:, c, 0, :], wqT[rows, :]).then_inc(s_w, 16)
                sp.dma_start(w_qk[:, c, 1, :], wkT[rows, :]).then_inc(s_w, 16)
                sp.dma_start(w_v[:, c, :], wvT[rows, :]).then_inc(s_w, 16)
                sp.dma_start(w_o[:, c, :], woT[rows, :]).then_inc(s_w, 16)
                sp.dma_start(b_qk[:, c:c + 1], bq[rows].unsqueeze(1)).then_inc(s_w, 16)
                sp.dma_start(b_qk[:, KC + c:KC + c + 1], bk[rows].unsqueeze(1)).then_inc(s_w, 16)
            for dst, src in ((g_tok, tok_g), (be_tok, tok_be), (b_v, bv), (b_o, bo), (g_ln, ln_g), (be_ln, ln_b)):
                sp.dma_start(dst[:, :], src.partition_broadcast(T)).then_inc(s_w, 16)

            def load_terms(b, g, s_ld):
                for r in range(TERMS):
                    for dst, part, row in ((QA, Q_PARTS[r], 0), (KA, K_PARTS[r], D)):
                        src = part_s[b, part, bass.ds(row + g * (HG * HD), HG * HD), :]
                        sp.dma_start(dst[r * HD:(r + 1) * HD, g % 2, :, :],
                                     src.rearrange("(hh d) q -> d hh q", d=HD)).then_inc(s_ld, 16)

            with sp.Fori(0, B) as b:
                with sp.Fori(0, NT // PGRP) as i:
                    k0 = b * NT + i * PGRP
                    for j in range(PGRP):
                        wait(sp, s_xT, k0)
                        sp.dma_start(xs[:, j, :], x_v[b, :, i * PGRP + j, :]).then_inc(s_x, 16)
                    for j in range(PGRP):
                        wait(sp, s_h, k0 + j + 1)
                        sp.dma_start(h_s[b, i * PGRP + j, :, :], hh[:, j, :]).then_inc(s_hst, 16)
                    for j in range(PGRP):
                        wait(sp, s_parts, k0 + j + 1)
                        for w in range(3):
                            dst = part_s[b, w, :, bass.ds((i * PGRP + j) * T, T)]
                            sp.dma_start(dst.rearrange("(m c) q -> c m q", c=128),
                                         parts[:, j, w, :, :]).then_inc(s_pst, 16)

                wait(sp, s_pst, 48 * NT * (b + 1))
                with sp.Fori(0, NG) as g:
                    gi = b * NG + g
                    wait(sp, s_mt, gi)
                    load_terms(b, g, s_ldm)
                    wait(sp, s_mc, gi + 1)
                    dst = max_s[b, :, bass.ds(g * HG, HG), :]
                    sp.dma_start(dst.rearrange("w hh (t q) -> (hh t) w q", q=T), mparts[:, :, :]).then_inc(s_cst, 16)

                wait(sp, s_cst, 16 * NG * (b + 1))

                def load_group(g):
                    load_terms(b, g, s_lda)
                    sp.dma_start(QA[MROW:KROWS, g % 2, :, :], max_s[b, :, bass.ds(g * HG, HG), :]).then_inc(s_lda, 16)

                def unit_output(g, c):
                    n = b * NCH + g * NC + c
                    wait(sp, s_ov, n + 1)
                    for j in range(HG):
                        lo = 2 * HD * j
                        sp.dma_start(Den[lo:lo + HD, :], Osb[lo + HD:lo + 2 * HD, :]).then_inc(s_dn, 16)
                    wait(sp, s_on, n + 1)
                    for j in range(HG):
                        dst = o_s[b, bass.ds(g * (HG * HD) + j * HD, HD), c * QC:(c + 1) * QC]
                        sp.dma_start(dst, On[2 * HD * j:2 * HD * j + HD, :]).then_inc(s_os, 16)

                load_group(0)
                with sp.Fori(0, NG - 1) as g:
                    wait(sp, s_lda, 16 * (2 * TERMS + 1) * (b * NG + g + 1))
                    wait(sp, s_pv, NT * (b * NCH + g * NC) + PV_AHEAD)
                    load_group(g + 1)
                    for c in range(NC):
                        unit_output(g, c)
                for c in range(NC):
                    unit_output(NG - 1, c)

                with sp.Fori(0, NT) as u:
                    k = b * NT + u
                    wait(sp, s_os, 16 * HG * NCH * (b + 1))
                    wait(sp, s_hst, 16 * NT * (b + 1))
                    wait(sp, s_s1, k)
                    sp.dma_start(oT[:, :, :], o_s[b, :, bass.ds(u * T, T)].rearrange("(m c) q -> c m q", c=128))\
                        .then_inc(s_el, 16)
                    sp.dma_start(hE[:, :], h_s[b, u, :, :]).then_inc(s_el, 16)
                    wait(sp, s_or, k + 1)
                    sp.dma_start(out_v[b, :, u, :], y2[:, :]).then_inc(s_ost, 16)
            wait(sp, s_ost, 16 * NT * B)

        @block.gpsimd
        def _(pool):
            pool.memset(ident[:, :], 0.0)
            pool.memset(mhalf[:, :], -0.5)
            pool.memset(eps[:, :], EPS)
            pool.drain()
            pool.affine_select(out=ident[:, :], in_=ident[:, :], compare_op=ALU.not_equal, fill=1.0,
                               base=0, pattern=[[-1, 128]], channel_multiplier=1).then_inc(s_id, 1)
            pool.wait_ge(s_w, 16 * WLOADS)
            with pool.Fori(0, B) as b:
                with pool.Fori(0, NT // PGRP) as i:
                    k0 = b * NT + i * PGRP
                    for j in range(PGRP):
                        pool.wait_ge(s_var, k0 + j + 1)
                        pool.tensor_tensor(rs[:, j, :], mv[:, j, 1:2], eps[0:T, :], ALU.add)
                    pool.drain()
                    for j in range(PGRP):
                        pool.tensor_tensor(rs[:, j, :], rs[:, j, :], mhalf[0:T, :], ALU.pow).then_inc(s_rs, 1)
                    for j in range(PGRP):
                        pool.wait_ge(s_nrm, k0 + j + 1)
                        pool.tensor_tensor(hp[:, j, :], hp[:, j, :], g_tok[:, :], ALU.mult)
                    pool.drain()
                    for j in range(PGRP):
                        pool.tensor_tensor(hp[:, j, :], hp[:, j, :], be_tok[:, :], ALU.add).then_inc(s_hp, 1)
                    for j in range(PGRP):
                        pool.wait_ge(s_var2, k0 + j + 1)
                        pool.tensor_tensor(rs2[:, j, :], mv2[:, j, 1:2], eps[0:T, :], ALU.add)
                    pool.drain()
                    for j in range(PGRP):
                        pool.tensor_tensor(rs2[:, j, :], rs2[:, j, :], mhalf[0:T, :], ALU.pow).then_inc(s_rs2, 1)
                with pool.Fori(0, NT) as u:
                    k = b * NT + u
                    for l in range(2):
                        pool.wait_ge(s_ev, 2 * k + l + 1)
                        pool.tensor_tensor(ers[:, :], emv[:, 1:2], eps[0:T, :], ALU.add)
                        pool.drain()
                        pool.tensor_tensor(ers[:, :], ers[:, :], mhalf[0:T, :], ALU.pow).then_inc(s_er, 1)
                    pool.wait_ge(s_y2, k + 1)
                    pool.tensor_tensor(y2[:, :], y2[:, :], g_ln[:, :], ALU.mult)
                    pool.drain()
                    pool.tensor_tensor(y2[:, :], y2[:, :], be_ln[:, :], ALU.add)
                    pool.drain()
                    pool.tensor_tensor(y2[:, :], y2[:, :], s1[:, :], ALU.add).then_inc(s_or, 1)

        @block.scalar
        def _(act):
            act.preload_act_table(ACT.Exp)
            with act.Fori(0, B) as b:
                with act.Fori(0, NT // PGRP) as i:
                    k0 = b * NT + i * PGRP
                    for j in range(PGRP):
                        act.wait_ge(s_hp, k0 + j + 1)
                        act.activation(ab[:, j, :], hp[:, j, :], ACT.Abs)
                        act.activation(ex[:, j, :], hp[:, j, :], ACT.Square, scale=RSQRT2)
                    act.drain()
                    for j in range(PGRP):
                        act.activation(ex[:, j, :], ex[:, j, :], ACT.Exp, scale=-1.0).then_inc(s_ex, 1)
                with act.Fori(0, NCH) as n:
                    first = (b * NCH + n) * SLOTS
                    for s in range(SLOTS):
                        act.wait_ge(s_sc, first + s + 1)
                        if s % 2 == 0:
                            act.wait_ge(s_pv, (b * NCH + n) * NT + s // 2 + 1)
                        act.activation(prob[:, s % PROBS, :, :], PS[0:T, 2 * (s % RING):2 * (s % RING) + 2, 0:QC],
                                       ACT.Exp, scale=SCALE).then_inc(s_pr, 1)

        @block.vector
        def _(dve):
            dve.memset(KA[96:KROWS, :, :, :].bitcast(f32), 0.0)
            dve.memset(xT[:, :, :], 1.0)
            dve.memset(Vst[:, :, :, :], 1.0)
            dve.memset(Den[:, :], 1.0)
            dve.drain()
            dve.memset(KA[96:KROWS, :, :, :], 1.0).then_inc(s_ones, 1)

            dve.wait_ge(s_w, 16 * WLOADS)

            def layer_stats(st, m, src, done):
                dve.bn_stats(st, src)
                dve.drain()
                dve.bn_aggr(m, st).then_inc(done, 1)

            with dve.Fori(0, B) as b:
                with dve.Fori(0, NT // PGRP) as i:
                    k0 = b * NT + i * PGRP
                    J = range(PGRP)
                    for j in J:
                        dve.wait_ge(s_xT, k0 + j + 1)
                        dve.tensor_copy(xT[0:RF, j, :], PS[0:RF, j, 0:T]).then_inc(s_xTs, 1)
                    for j in J:
                        dve.wait_ge(s_tok, k0 + j + 1)
                        dve.bn_stats(stat[:, j, :], PS[0:T, j, 0:D])
                    dve.drain()
                    for j in J:
                        dve.bn_aggr(mv[:, j, :], stat[:, j, :]).then_inc(s_var, 1)
                    for j in J:
                        dve.wait_ge(s_rs, k0 + j + 1)
                        dve.tensor_scalar(hp[:, j, :], PS[0:T, j, 0:D], mv[:, j, 0:1], rs[:, j, :],
                                          ALU.subtract, ALU.mult).then_inc(s_nrm, 1)
                    for j in J:
                        dve.wait_ge(s_ex, k0 + j + 1)
                        dve.tensor_scalar(tt[:, j, :], ab[:, j, :], ERF_P * RSQRT2, 1.0, ALU.mult, ALU.add)
                    dve.drain()
                    for j in J:
                        dve.reciprocal(tt[:, j, :], tt[:, j, :])
                    dve.drain()
                    for j in J:
                        dve.tensor_scalar(qq[:, j, :], tt[:, j, :], ERF_A[4], None, ALU.mult)
                    for a in (ERF_A[3], ERF_A[2], ERF_A[1], ERF_A[0]):
                        dve.drain()
                        for j in J:
                            dve.scalar_tensor_tensor(out=qq[:, j, :], in0=qq[:, j, :], scalar=a, in1=tt[:, j, :],
                                                     op0=ALU.add, op1=ALU.mult)
                    dve.drain()
                    for j in J:
                        dve.tensor_tensor(qq[:, j, :], qq[:, j, :], ex[:, j, :], ALU.mult)
                    dve.drain()
                    for j in J:
                        dve.scalar_tensor_tensor(out=qq[:, j, :], in0=ab[:, j, :], scalar=0.5, in1=qq[:, j, :],
                                                 op0=ALU.mult, op1=ALU.mult)
                    dve.drain()
                    dve.wait_ge(s_hst, 16 * k0)
                    for j in J:
                        dve.scalar_tensor_tensor(out=hh[:, j, :], in0=hp[:, j, :], scalar=0.0, in1=qq[:, j, :],
                                                 op0=ALU.max, op1=ALU.subtract).then_inc(s_h, 1)
                    dve.drain()
                    for j in J:
                        dve.bn_stats(stat2[:, j, :], hh[:, j, :])
                    dve.drain()
                    for j in J:
                        dve.bn_aggr(mv2[:, j, :], stat2[:, j, :]).then_inc(s_var2, 1)
                    for j in J:
                        dve.wait_ge(s_rs2, k0 + j + 1)
                        dve.tensor_scalar(tt[:, j, :], hh[:, j, :], mv2[:, j, 0:1], rs2[:, j, :],
                                          ALU.subtract, ALU.mult).then_inc(s_z, 1)
                    for j in J:
                        dve.wait_ge(s_zT, k0 + j + 1)
                        dve.tensor_copy(zT[:, j, :, :], PS[:, j, 0:KC * T].rearrange("p (c t) -> p c t", c=KC))\
                           .then_inc(s_zTs, 1)
                    for j in J:
                        dve.wait_ge(s_qk, k0 + j + 1)
                        bias = b_qk[:, :].unsqueeze(2).broadcast_to([128, 2 * KC, T])
                        dve.tensor_tensor(fq[:, j, :, :], PS[:, j, 0:2 * KC * T].rearrange("p (c t) -> p c t", t=T),
                                          bias, ALU.add).then_inc(s_f, 1)
                    dve.drain()
                    dve.wait_ge(s_pst, 48 * k0)
                    for w in range(3):
                        for j in J:
                            ins = dve.tensor_copy(parts[:, j, w, :, :], fq[:, j, :, :])
                            if w == 2:
                                ins.then_inc(s_parts, 1)
                        if w < 2:
                            dve.drain()
                            for j in J:
                                dve.tensor_tensor(fq[:, j, :, :], fq[:, j, :, :], parts[:, j, w, :, :], ALU.subtract)
                            dve.drain()
                    for j in J:
                        dve.wait_ge(s_v, k0 + j + 1)
                        dve.tensor_tensor(Vb[:, b % 2, i * PGRP + j, :], PS[0:T, j, 0:D], b_v[:, :], ALU.add)\
                           .then_inc(s_vb, 1)
                    dve.drain()

                with dve.Fori(0, NG) as g:
                    with dve.Fori(0, HG * NT // 2) as i:
                        for s in range(2):
                            n = (b * NG + g) * HG * NT + 2 * i + s
                            dve.wait_ge(s_ms, n + 1)
                            dve.reduce_max(mx[:, bass.ds(2 * i + s, 1)], PS[0:T, 3 * s:3 * s + 3, 0:QC], AX.XY)\
                               .then_inc(s_mx, 1)
                    dve.wait_ge(s_mt, b * NG + g + 1)
                    dve.tensor_scalar(mf[:, :], PS[0:HG * NT, MISC, 0:T], -1.0, None, ALU.mult).then_inc(s_mtT, 1)
                    dve.drain()
                    dve.wait_ge(s_cst, 16 * (b * NG + g))
                    for w in range(3):
                        ins = dve.tensor_copy(mparts[:, w, :], mf[:, :])
                        if w == 2:
                            ins.then_inc(s_mc, 1)
                        dve.drain()
                        if w < 2:
                            dve.tensor_tensor(mf[:, :], mf[:, :], mparts[:, w, :], ALU.subtract)
                            dve.drain()

                with dve.Fori(0, NCH) as c:
                    n = b * NCH + c
                    g = c // NC
                    dve.wait_ge(s_pv, n * NT + PV_AHEAD)
                    src = Vb[:, b % 2, :, bass.ds(g * (HG * HD), HG * HD)].rearrange("p t (h d) -> p t h d", d=HD)
                    dve.tensor_scalar(Vst[:, :, :, 0:HD], src, 1.0, None, ALU.mult).then_inc(s_vst, 1)
                    dve.wait_ge(s_dn, 64 * n)
                    dve.wait_ge(s_pv, (n + 1) * NT + PV_AHEAD)
                    dve.tensor_copy(Osb[:, :], PS[:, PVB, 0:QC]).then_inc(s_ov, 1)
                    dve.wait_ge(s_dn, 64 * (n + 1))
                    dve.wait_ge(s_os, 64 * n)
                    dve.reciprocal(On[:, :], Den[:, :])
                    dve.drain()
                    dve.tensor_tensor(On[:, :], On[:, :], Osb[:, :], ALU.mult).then_inc(s_on, 1)

                with dve.Fori(0, NT) as u:
                    k = b * NT + u
                    dve.wait_ge(s_or, k)
                    dve.wait_ge(s_ost, 16 * k)
                    dve.wait_ge(s_el, 32 * (k + 1))
                    dve.wait_ge(s_eo, k + 1)
                    dve.tensor_tensor(s1[:, :], PS[0:T, MISC, 0:D], hE[:, :], ALU.add).then_inc(s_s1, 1)
                    dve.drain()
                    dve.tensor_tensor(s1[:, :], s1[:, :], b_o[:, :], ALU.add)
                    for l, (src, dst) in enumerate(((s1, y1), (y1, y2))):
                        dve.drain()
                        layer_stats(estat[:, :], emv[:, :], src[:, :], s_ev)
                        dve.wait_ge(s_er, 2 * k + l + 1)
                        ins = dve.tensor_scalar(dst[:, :], src[:, :], emv[:, 0:1], ers[:, :], ALU.subtract, ALU.mult)
                        if l == 1:
                            ins.then_inc(s_y2, 1)

        @block.tensor
        def _(pe):
            pe.wait_ge(s_w, 16 * WLOADS)
            pe.wait_ge(s_id, 1)
            pe.wait_ge(s_ones, 1)
            pe.sem_inc(s_pv, PV_AHEAD)
            pe.sem_inc(s_mx, 2)
            with pe.Fori(0, B) as b:
                with pe.Fori(0, NT // PGRP) as i:
                    k0 = b * NT + i * PGRP
                    J = range(PGRP)
                    pe.wait_ge(s_vb, k0)
                    for j in J:
                        pe.wait_ge(s_x, 16 * (k0 + PGRP))
                        pe.transpose(PS[0:RF, j, 0:T], xs[:, j, :], ident[0:T, 0:T]).then_inc(s_xT, 1)
                    for j in J:
                        pe.wait_ge(s_xTs, k0 + j + 1)
                        pe.matmul(PS[0:T, j, 0:D], xT[:, j, :], w_tok[:, :], start=True, stop=True).then_inc(s_tok, 1)
                    for j in J:
                        pe.wait_ge(s_z, k0 + j + 1)
                        for c in range(KC):
                            last = pe.transpose(PS[:, j, c * T:(c + 1) * T], tt[:, j, c * 128:(c + 1) * 128],
                                                ident[0:T, 0:T])
                        last.then_inc(s_zT, 1)
                    for j in J:
                        pe.wait_ge(s_zTs, k0 + j + 1)
                        for w in range(2):
                            for m in range(KC):
                                o = (w * KC + m) * T
                                for c in range(KC):
                                    last = pe.matmul(PS[:, j, o:o + T], w_qk[:, c, w, m * 128:(m + 1) * 128],
                                                     zT[:, j, c, :], start=(c == 0), stop=(c == KC - 1))
                        last.then_inc(s_qk, 1)
                    for j in J:
                        pe.wait_ge(s_f, k0 + j + 1)
                        for c in range(KC):
                            last = pe.matmul(PS[0:T, j, 0:D], zT[:, j, c, :], w_v[:, c, :],
                                             start=(c == 0), stop=(c == KC - 1))
                        last.then_inc(s_v, 1)

                with pe.Fori(0, NG) as g:
                    pe.wait_ge(s_ldm, 16 * 2 * TERMS * (b * NG + g + 1))
                    wait(pe, s_vb, NT * (b + 1))
                    with pe.Fori(0, HG * NT // 2) as i:
                        for s in range(2):
                            n = (b * NG + g) * HG * NT + 2 * i + s
                            pe.wait_ge(s_mx, n + 1)
                            col = ((2 * i) // NT) * S + ((2 * i) % NT + s) * T
                            qa = QA[0:MROW, g % 2, :, :].rearrange("k h q -> k (h q)")
                            ka = KA[0:MROW, g % 2, (2 * i) // NT, :]
                            for c in range(NC):
                                last = pe.matmul(PS[0:T, 3 * s + c, 0:QC], qa[:, bass.ds(col, T)],
                                                 ka[:, c * QC:(c + 1) * QC], start=True, stop=True)
                            last.then_inc(s_ms, 1)
                    wait(pe, s_mx, (b * NG + g + 1) * HG * NT + 2)
                    pe.transpose(PS[0:HG * NT, MISC, 0:T], mx[:, :], ident[0:T, 0:T]).then_inc(s_mt, 1)
                pe.wait_ge(s_mtT, NG * (b + 1))

                def scores(c, s):
                    g, q = c // NC, c % NC
                    n = b * NCH + c
                    t, pair = s // 2, s % 2
                    pe.wait_ge(s_pr, n * SLOTS + s - RING + 1) if s >= RING else None
                    for e in range(2):
                        hd = 2 * pair + e
                        last = pe.matmul(PS[0:T, 2 * (s % RING) + e, 0:QC], KA[:, g % 2, hd, t * T:(t + 1) * T],
                                         QA[:, g % 2, hd, bass.ds(q * QC, QC)], start=True, stop=True)
                    last.then_inc(s_sc, 1)

                def attend(c, t):
                    n = b * NCH + c
                    if t == 0:
                        pe.wait_ge(s_vst, n + 1)
                        pe.wait_ge(s_ov, n)
                    pe.wait_ge(s_pr, n * SLOTS + 2 * t + 2)
                    for hd in range(HG):
                        lo = 2 * HD * hd
                        last = pe.matmul(PS[lo:lo + 2 * HD, PVB, 0:QC], Vst[:, t, hd, :],
                                         prob[:, (2 * t + hd // 2) % PROBS, hd % 2, :],
                                         start=(t == 0), stop=(t == NT - 1))
                    last.then_inc(s_pv, 1)

                def unit(c, last):
                    for t in range(NT):
                        for s in (2 * t + RING, 2 * t + RING + 1):
                            if s < SLOTS:
                                scores(c, s)
                            elif not last:
                                if s == SLOTS:
                                    pe.wait_ge(s_lda, 16 * (2 * TERMS + 1) * (b * NG + (c + 1) // NC + 1))
                                pe.wait_ge(s_pr, (b * NCH + c) * SLOTS + s - RING + 1)
                                scores(c + 1, s - SLOTS)
                        attend(c, t)

                pe.wait_ge(s_lda, 16 * (2 * TERMS + 1) * (b * NG + 1))
                wait(pe, s_pr, b * NCH * SLOTS)
                for s in range(RING):
                    scores(0, s)
                with pe.Fori(0, NCH - 1) as c:
                    unit(c, False)
                unit(NCH - 1, True)

                with pe.Fori(0, NT) as u:
                    k = b * NT + u
                    pe.wait_ge(s_el, 32 * (k + 1))
                    pe.wait_ge(s_s1, k)
                    for c in range(KC):
                        last = pe.matmul(PS[0:T, MISC, 0:D], oT[:, c, :], w_o[:, c, :],
                                         start=(c == 0), stop=(c == KC - 1))
                    last.then_inc(s_eo, 1)


_OUT = ((8, 1500, 256), 'float32')


def kernel(**inputs):
    import numpy as _np
    import concourse.bacc as _bacc
    from concourse import mybir as _mybir
    from concourse.bass_utils import run_bass_kernel_spmd as _run

    given = {
        "x": inputs["x"],
        "tok_wT": _np.asarray(inputs["L0_tok_W"]).T, "tok_b": inputs["L0_tok_b"],
        "tok_g": inputs["L0_tok_ln_gamma"], "tok_be": inputs["L0_tok_ln_beta"],
        "wqT": _np.asarray(inputs["L0_attn_Wq"]).T, "bq": inputs["L0_attn_bq"],
        "wkT": _np.asarray(inputs["L0_attn_Wk"]).T, "bk": inputs["L0_attn_bk"],
        "wvT": _np.asarray(inputs["L0_attn_Wv"]).T, "bv": inputs["L0_attn_bv"],
        "woT": _np.asarray(inputs["L0_attn_Wo"]).T, "bo": inputs["L0_attn_bo"],
        "ln_g": inputs["L0_ffn_ln_g"], "ln_b": inputs["L0_ffn_ln_b"],
    }
    nc = _bacc.Bacc("TRN2", target_bir_lowering=False, num_devices=1)
    arrays, args = {}, []
    for name, value in given.items():
        a = _np.ascontiguousarray(value)
        arrays[f"in_{name}"] = a
        args.append(nc.dram_tensor(f"in_{name}", a.shape, _mybir.dt.from_np(a.dtype), kind="ExternalInput").ap())
    args.append(nc.dram_tensor("out_0", _OUT[0], _mybir.dt.from_np(_np.dtype(_OUT[1])), kind="ExternalOutput").ap())
    audio_tower(nc, *args)
    r = _run(nc, [arrays], core_ids=[0])
    return r.results[0]["out_0"]
```

```python
import concourse.bass as bass
from concourse import mybir
from contextlib import ExitStack


RMAX = bass.bass_isa.ReduceOp.max


def audio_tower(nc, x, tok_wT, tok_b, tok_g, tok_be, wqT, bq, wkT, bk, wvT, bv, woT, bo, ln_g, ln_b, out):
    f32, bf16, i32 = mybir.dt.float32, mybir.dt.bfloat16, mybir.dt.int32
    ALU, ACT, AX = mybir.AluOpType, mybir.ActivationFunctionType, mybir.AxisListType

    B = x.shape[0]
    RF, D = tok_wT.shape
    S = x.shape[1] * x.shape[3]
    H = 16
    HD = D // H
    T = 125
    NT = S // T
    QC = 500
    NC = S // QC
    HG = 4
    NG = H // HG
    NCH = NG * NC
    KC = D // 128
    EPS = 1e-5
    SCALE = float(HD) ** -0.5
    assert T * NT == S and QC * NC == S and NCH == NT

    K_PARTS = [0, 1, 2, 0, 1, 0, 2]
    Q_PARTS = [0, 0, 0, 1, 1, 2, 1]
    TERMS = len(K_PARTS)
    MROW = TERMS * HD
    KROWS = MROW + 3

    PGRP = 4
    RING = 3
    PROBS = 6
    SLOTS = 2 * NT
    AHEAD = PROBS // 2
    LEAD = NT + PGRP
    VBUF = 3
    NU = B * NCH
    BL, CL = divmod(NU - LEAD, NCH)
    RC = 2 * NT - LEAD + 1
    assert BL == B - 2 and NC <= CL < NCH
    GLOADS = 2 * TERMS + 1
    BOUND = 60.0

    ERF_P = 0.3275911
    ERF_A = [0.254829592, -0.284496736, 1.421413741, -1.453152027, 1.061405429]
    RSQRT2 = 0.5 ** 0.5

    h_s = nc.dram_tensor("h_scratch", [B, NT, T, D], f32, kind="Internal").ap()
    part_s = nc.dram_tensor("qk_parts_scratch", [B, 3, 2 * D, S], bf16, kind="Internal").ap()
    max_t = nc.dram_tensor("minus_max_scratch", [B, 3, H, S], bf16, kind="Internal")
    max_s = max_t.ap()
    o_s = nc.dram_tensor("attended_scratch", [B, D, S], f32, kind="Internal").ap()
    out_v = out.rearrange("b (p u) d -> b p u d", u=NT)

    with ExitStack() as ctx:
        def sb(name, shape, dt=f32):
            return ctx.enter_context(nc.sbuf_tensor(name, shape, dt))

        ident = sb("ident", [128, 128])
        w_tok = sb("w_tok", [RF + 1, D])
        w_qk = sb("w_qk", [128, KC, 2, D])
        w_v = sb("w_v", [128, KC, D])
        w_o = sb("w_o", [128, KC, D])
        b_qk = sb("b_qk", [128, 2 * KC])
        g_tok, be_tok, b_v, b_o, g_ln, be_ln = (sb(n, [T, D]) for n in
                                                ("g_tok", "be_tok", "b_v", "b_o", "g_ln", "be_ln"))
        mhalf = sb("mhalf", [128, 1])
        eps = sb("eps", [128, 1])
        head_sel = sb("head_sel", [128, 128 // HD], bf16)
        xT = sb("xT", [RF + 1, PGRP, T])
        hp = sb("hp", [T, PGRP, D])
        ab = sb("ab", [T, PGRP, D])
        ex = sb("ex", [T, PGRP, D])
        tt = sb("tt", [T, PGRP, D])
        qq = sb("qq", [T, PGRP, D])
        hh = sb("hh", [T, PGRP, D])
        zT = sb("zT", [128, PGRP, KC, T])
        fq = sb("fq", [128, PGRP, 2 * KC, T])
        sq = sb("sq", [128, PGRP, 2 * KC, T], bf16)
        parts = sb("parts", [128, PGRP, 3, 2 * KC, T], bf16)
        stat, mv, rs = sb("stat", [T, PGRP, 6]), sb("mv", [T, PGRP, 2]), sb("rs", [T, PGRP, 1])
        stat2, mv2, rs2 = sb("stat2", [T, PGRP, 6]), sb("mv2", [T, PGRP, 2]), sb("rs2", [T, PGRP, 1])
        norms = sb("norms", [T, VBUF, NT, 2 * H])
        nmax, nall = sb("nmax", [T, 2 * H]), sb("nall", [T, 2 * H])
        nprod = sb("nprod", [1, H + 1])
        flags = sb("flags", [1, B + 1], i32)
        QA = sb("QA", [KROWS, 2, HG, S], bf16)
        KA = sb("KA", [KROWS, 2, HG, S], bf16)
        Vb = sb("Vb", [T, VBUF, NT, D])
        Vst = sb("Vst", [T, NT, HG, 2 * HD])
        prob = sb("prob", [T, PROBS, 2, QC])
        Osb = sb("Osb", [128, QC])
        Den = sb("Den", [128, QC])
        On = sb("On", [128, QC])
        mx = sb("mx", [T, HG * NT])
        mf = sb("mf", [HG * NT, T])
        mparts = sb("mparts", [HG * NT, 3, T], bf16)
        oT = sb("oT", [128, KC, T])
        hE, s1, y2 = sb("hE", [T, D]), sb("s1", [T, D]), sb("y2", [T, D])
        estat, emv, ers = sb("estat", [T, 6]), sb("emv", [T, 2]), sb("ers", [T, 2])

        PS = ctx.enter_context(nc.psum_tensor("PS", [128, 8, 512], f32))
        PVB, MISC = 6, 7

        ONE = 1
        credits = []

        def sem(name, credit=ONE):
            s = ctx.enter_context(nc.semaphore(name))
            credits.append((s, credit))
            return s

        s_w, s_id, s_zero, s_cred, s_zeros, s_fill, s_seen = (sem(n, 0) for n in (
            "s_w", "s_id", "s_zero", "s_cred", "s_zeros", "s_fill", "s_seen"))
        s_x, s_tok, s_var, s_rs, s_nrm, s_hp, s_ex, s_h, s_hb, s_hst = (sem(n) for n in (
            "s_x", "s_tok", "s_var", "s_rs", "s_nrm", "s_hp", "s_ex", "s_h", "s_hb", "s_hst"))
        s_var2, s_rs2, s_z, s_zT, s_zTs, s_qk, s_f, s_sq, s_parts, s_pst, s_v, s_vb, s_ns, s_nm = (sem(n) for n in (
            "s_var2", "s_rs2", "s_z", "s_zT", "s_zTs", "s_qk", "s_f", "s_sq", "s_parts", "s_pst", "s_v", "s_vb",
            "s_ns", "s_nm"))
        s_nmax, s_nall, s_flag = sem("s_nmax"), sem("s_nall"), sem("s_flag")
        s_ldm, s_ms, s_mt, s_mtT, s_mc, s_cst, s_rl = (sem(n) for n in (
            "s_ldm", "s_ms", "s_mt", "s_mtT", "s_mc", "s_cst", "s_rl"))
        s_mx = sem("s_mx", 2)
        s_lda, s_sc, s_vst, s_ov, s_dn, s_on, s_os = (sem(n) for n in (
            "s_lda", "s_sc", "s_vst", "s_ov", "s_dn", "s_on", "s_os"))
        s_pr, s_pv = sem("s_pr", RING), sem("s_pv", AHEAD)
        s_el, s_eo, s_s1, s_ev, s_er, s_y2, s_or, s_ost = (sem(n) for n in (
            "s_el", "s_eo", "s_s1", "s_ev", "s_er", "s_y2", "s_or", "s_ost"))
        block = ctx.enter_context(nc.Block())

        def wait(eng, sem_, value):
            eng.wait_ge(sem_, value)
            eng.sem_inc(s_seen, 1)

        WLOADS = 2 + KC * 6 + 6
        ZCOLS = 900
        ZLOADS = B * 3 * H * S // (128 * ZCOLS)
        assert ZLOADS * 128 * ZCOLS == B * 3 * H * S


        @block.sync
        def _(sp):
            sp.dma_start(w_tok[0:RF, :], tok_wT).then_inc(s_w, 16)
            sp.dma_start(w_tok[RF:RF + 1, :], tok_b.unsqueeze(0)).then_inc(s_w, 16)
            for c in range(KC):
                rows = slice(c * 128, (c + 1) * 128)
                sp.dma_start(w_qk[:, c, 0, :], wqT[rows, :]).then_inc(s_w, 16)
                sp.dma_start(w_qk[:, c, 1, :], wkT[rows, :]).then_inc(s_w, 16)
                sp.dma_start(w_v[:, c, :], wvT[rows, :]).then_inc(s_w, 16)
                sp.dma_start(w_o[:, c, :], woT[rows, :]).then_inc(s_w, 16)
                sp.dma_start(b_qk[:, c:c + 1], bq[rows].unsqueeze(1)).then_inc(s_w, 16)
                sp.dma_start(b_qk[:, KC + c:KC + c + 1], bk[rows].unsqueeze(1)).then_inc(s_w, 16)
            for dst, src in ((g_tok, tok_g), (be_tok, tok_be), (b_v, bv), (b_o, bo), (g_ln, ln_g), (be_ln, ln_b)):
                sp.dma_start(dst[:, :], src.partition_broadcast(T)).then_inc(s_w, 16)
            sp.wait_ge(s_cred, 1)
            sp.wait_ge(s_zeros, 1)
            sp.wait_ge(s_fill, 1)
            flat = max_s.rearrange("b w h q -> (b w h q)").rearrange("(i p c) -> i p c", p=128, c=ZCOLS)
            for i in range(ZLOADS):
                sp.dma_start(flat[i, :, :], On[:, 0:ZCOLS // 2].bitcast(bf16)).then_inc(s_zero, 16)

            def load_x(k, j):
                k = k % (B * NT)
                sp.dma_start(xT[0:RF, j, :], x[k // NT, k % NT, :, :]).then_inc(s_x, 16)

            def store_h(k, j):
                wait(sp, s_hb, ONE + k + 1)
                sp.dma_start(h_s[k // NT, k % NT, :, :], hh[:, j, :]).then_inc(s_hst, 16)

            def store_parts(k, j):
                wait(sp, s_parts, ONE + k + 1)
                for w in range(3):
                    dst = part_s[k // NT, w, :, bass.ds((k % NT) * T, T)]
                    sp.dma_start(dst.rearrange("(m c) q -> c m q", c=128), parts[:, j, w, :, :]).then_inc(s_pst, 16)

            def load_term(b, g, buf, r, s_ld):
                for dst, part, row in ((QA, Q_PARTS[r], 0), (KA, K_PARTS[r], D)):
                    src = part_s[b, part, bass.ds(row + g * (HG * HD), HG * HD), :]
                    sp.dma_start(dst[r * HD:(r + 1) * HD, buf, :, :],
                                 src.rearrange("(hh d) q -> d hh q", d=HD)).then_inc(s_ld, 16)

            def load_max(b, g, buf, s_ld):
                sp.dma_start(QA[MROW:KROWS, buf, :, :], max_s[b, :, bass.ds(g * HG, HG), :]).then_inc(s_ld, 16)

            def load_ready(G, p):
                wait(sp, s_lda, ONE + 16 * GLOADS * G)
                wait(sp, s_pst, ONE + 48 * NT * (G // NG + 1 if p else B))

            def denominators(n):
                wait(sp, s_ov, ONE + n + 1)
                for j in range(HG):
                    lo = 2 * HD * j
                    sp.dma_start(Den[lo:lo + HD, :], Osb[lo + HD:lo + 2 * HD, :]).then_inc(s_dn, 16)

            def store_attended(n):
                wait(sp, s_on, ONE + n + 1)
                b, c = n // NCH, n % NCH
                g, q = c // NC, c % NC
                for j in range(HG):
                    dst = o_s[b, bass.ds(g * (HG * HD) + j * HD, HD), bass.ds(q * QC, QC)]
                    sp.dma_start(dst, On[2 * HD * j:2 * HD * j + HD, :]).then_inc(s_os, 16)

            def load_out(e):
                b, u = e // NT, e % NT
                wait(sp, s_os, ONE + 16 * HG * NCH * (b + 1))
                wait(sp, s_s1, ONE + e)
                sp.dma_start(oT[:, :, :], o_s[b, :, bass.ds(u * T, T)].rearrange("(m c) q -> c m q", c=128))\
                    .then_inc(s_el, 16)
                sp.dma_start(hE[:, :], h_s[b, u, :, :]).then_inc(s_el, 16)

            def store_out(e):
                wait(sp, s_or, ONE + e + 1)
                sp.dma_start(out_v[e // NT, :, e % NT, :], y2[:, :]).then_inc(s_ost, 16)

            def seam(b):
                wait(sp, s_flag, ONE + b + 1)
                flag = sp.value_load(flags[0:1, bass.ds(b, 1)], min_val=0, max_val=1)
                with sp.If(flag != 0):
                    wait(sp, s_sc, ONE + SLOTS * NCH * b)
                    wait(sp, s_lda, ONE + 16 * GLOADS * (b * NG + 1))
                    with sp.Fori(0, NG) as g:
                        wait(sp, s_mt, ONE + b * NG + g)
                        for r in range(TERMS):
                            load_term(b, g, 1, r, s_ldm)
                        wait(sp, s_mc, ONE + b * NG + g + 1)
                        dst = max_s[b, :, bass.ds(g * HG, HG), :]
                        sp.dma_start(dst.rearrange("w hh (t q) -> (hh t) w q", q=T), mparts[:, :, :])\
                          .then_inc(s_cst, 16)
                    wait(sp, s_cst, ONE + 16 * NG * (b + 1))
                    load_max(b, 0, 0, s_rl)
                with sp.Else():
                    sp.sem_inc(s_ldm, 16 * 2 * TERMS * NG)
                    sp.sem_inc(s_cst, 16 * NG)
                    sp.sem_inc(s_rl, 16)

            def unit(b, c, first, p, e, load, seam_before=False):
                n = b * NCH + c
                k = n + LEAD
                if e and not seam_before:
                    load_out(n - NT)
                if not first:
                    denominators(n - 1)
                if load is not None:
                    G = b * NG + c // NC + 1
                    if load == 0:
                        load_ready(G, p)
                    G = G % (B * NG)
                    for r in (range(4), range(4, TERMS))[load]:
                        load_term(G // NG, G % NG, G % 2, r, s_lda)
                    if load == 1:
                        load_max(G // NG, G % NG, G % 2, s_lda)
                if not first:
                    store_attended(n - 1)
                if e and seam_before:
                    load_out(n - NT)
                if p:
                    wait(sp, s_tok, ONE + k + 1)
                    load_x(k + 1, 0)
                if p and not first:
                    store_parts(k - 1, 0)
                if p:
                    store_h(k, 0)
                if e:
                    store_out(n - NT)

            def group(b, g, first, p, e, seam_before=False):
                for c in range(NC):
                    unit(b, g * NC + c, first and c == 0, p, e, c if c < 2 else None, seam_before and c == 0)

            with sp.Fori(0, LEAD // PGRP) as i:
                for j in range(PGRP):
                    wait(sp, s_tok, ONE + i * PGRP)
                    load_x(i * PGRP + j, j)
                for j in range(PGRP):
                    store_h(i * PGRP + j, j)
                for j in range(PGRP):
                    store_parts(i * PGRP + j, j)
            sp.wait_ge(s_tok, ONE + LEAD)
            load_x(LEAD, 0)
            sp.wait_ge(s_zero, 16 * ZLOADS)
            sp.wait_ge(s_pst, ONE + 48 * NT)
            for r in range(TERMS):
                load_term(0, 0, 0, r, s_lda)
            load_max(0, 0, 0, s_lda)
            seam(0)
            group(0, 0, True, True, False)
            with sp.Fori(1, NG) as g:
                group(0, g, False, True, False)
            with sp.Fori(1, BL) as b:
                seam(b)
                group(b, 0, False, True, True, True)
                with sp.Fori(1, NG) as g:
                    group(b, g, False, True, True)
            seam(BL)
            group(BL, 0, False, True, True, True)
            for c in range(NC, NCH):
                if c == CL:
                    store_parts(B * NT - 1, 0)
                unit(BL, c, False, c < CL, True, c % NC if c % NC < 2 else None)
            seam(B - 1)
            group(B - 1, 0, False, False, True, True)
            with sp.Fori(1, NG) as g:
                group(B - 1, g, False, False, True)
            denominators(NU - 1)
            store_attended(NU - 1)
            with sp.Fori(NU - NT, NU) as e:
                load_out(e)
                store_out(e)
            sp.wait_ge(s_ost, ONE + 16 * NT * B)
            sp.wait_ge(s_hst, ONE + 16 * NT * B)
            sp.wait_ge(s_pst, ONE + 48 * NT * B)
            sp.wait_ge(s_os, ONE + 16 * HG * NU)
            sp.wait_ge(s_cst, ONE + 16 * NG * B)
            sp.wait_ge(s_x, ONE + 16 * (NT * B + 1))
            sp.wait_ge(s_lda, ONE + 16 * GLOADS * (NG * B + 1))

        @block.gpsimd
        def _(pool):
            for s, credit in credits:
                if credit:
                    pool.sem_inc(s, credit)
            pool.sem_inc(s_cred, 1)
            pool.memset(ident[:, :], 0.0)
            pool.memset(mhalf[:, :], -0.5)
            pool.memset(eps[:, :], EPS)
            pool.memset(head_sel[:, :], 1.0)
            pool.drain()
            pool.affine_select(out=ident[:, :], in_=ident[:, :], compare_op=ALU.not_equal, fill=1.0,
                               base=0, pattern=[[-1, 128]], channel_multiplier=1)
            pool.affine_select(out=head_sel[:, :], in_=head_sel[:, :], compare_op=ALU.is_ge, fill=0.0,
                               base=0, pattern=[[-HD, 128 // HD]], channel_multiplier=1)
            pool.drain()
            pool.affine_select(out=head_sel[:, :], in_=head_sel[:, :], compare_op=ALU.is_ge, fill=0.0,
                               base=HD - 1, pattern=[[HD, 128 // HD]], channel_multiplier=-1).then_inc(s_id, 1)
            pool.wait_ge(s_w, 16 * WLOADS)

            def rsqrt(k, J, s_in, m, r, s_out):
                for j in J:
                    pool.wait_ge(s_in, ONE + k + j + 1)
                    pool.tensor_tensor(r[:, j, :], m[:, j, 1:2], eps[0:T, :], ALU.add)
                pool.drain()
                for j in J:
                    pool.tensor_tensor(r[:, j, :], r[:, j, :], mhalf[0:T, :], ALU.pow).then_inc(s_out, 1)

            def tok_affine(k, J):
                for j in J:
                    pool.wait_ge(s_nrm, ONE + k + j + 1)
                    pool.tensor_tensor(hp[:, j, :], hp[:, j, :], g_tok[:, :], ALU.mult)
                pool.drain()
                for j in J:
                    pool.tensor_tensor(hp[:, j, :], hp[:, j, :], be_tok[:, :], ALU.add).then_inc(s_hp, 1)

            def add_bias(k, J):
                for j in J:
                    pool.wait_ge(s_z, ONE + k + j + 1)
                    pool.tensor_tensor(hh[:, j, :], hh[:, j, :], b_o[:, :], ALU.add).then_inc(s_hb, 1)

            def squares(k, J):
                for j in J:
                    wait(pool, s_ns, ONE + k)
                    pool.wait_ge(s_f, ONE + k + j + 1)
                    pool.tensor_tensor(sq[:, j, :, :], fq[:, j, :, :], fq[:, j, :, :], ALU.mult).then_inc(s_sq, 1)

            def out_rsqrt(e):
                wait(pool, s_ev, ONE + e + 1)
                pool.tensor_scalar(ers[:, 0:1], emv[:, 1:2], 1.0 + EPS, EPS * EPS, ALU.mult, ALU.add)
                pool.drain()
                pool.tensor_tensor(ers[:, 1:2], ers[:, 0:1], mhalf[0:T, :], ALU.pow).then_inc(s_er, 1)

            def out_affine(e):
                pool.wait_ge(s_y2, ONE + e + 1)
                pool.tensor_tensor(y2[:, :], y2[:, :], g_ln[:, :], ALU.mult)
                pool.drain()
                pool.tensor_tensor(y2[:, :], y2[:, :], be_ln[:, :], ALU.add)
                pool.drain()
                pool.tensor_tensor(y2[:, :], y2[:, :], s1[:, :], ALU.add).then_inc(s_or, 1)

            def range_of(b):
                wait(pool, s_nmax, ONE + b + 1)
                pool.partition_all_reduce(nall[:, :], nmax[:, :], T, RMAX).then_inc(s_nall, 1)

            def unit(b, c, first, p, e):
                n = b * NCH + c
                k = n + LEAD
                if p:
                    rsqrt(k, [0], s_var, mv, rs, s_rs)
                    tok_affine(k, [0])
                if p and not first:
                    squares(k - 1, [0])
                if e:
                    out_rsqrt(n - NT)
                if p:
                    rsqrt(k, [0], s_var2, mv2, rs2, s_rs2)
                    add_bias(k, [0])
                if e:
                    out_affine(n - NT)

            with pool.Fori(0, LEAD // PGRP) as i:
                k, J = i * PGRP, range(PGRP)
                rsqrt(k, J, s_var, mv, rs, s_rs)
                tok_affine(k, J)
                rsqrt(k, J, s_var2, mv2, rs2, s_rs2)
                add_bias(k, J)
                squares(k, J)
            range_of(0)
            unit(0, 0, True, True, False)
            with pool.Fori(1, RC) as c:
                unit(0, c, False, True, False)
            range_of(1)
            with pool.Fori(RC, NCH) as c:
                unit(0, c, False, True, False)
            with pool.Fori(1, BL) as b:
                with pool.Fori(0, RC) as c:
                    unit(b, c, False, True, True)
                range_of(b + 1)
                with pool.Fori(RC, NCH) as c:
                    unit(b, c, False, True, True)
            with pool.Fori(0, CL) as c:
                unit(BL, c, False, True, True)
            squares(B * NT - 1, [0])
            range_of(B - 1)
            with pool.Fori(CL, NCH) as c:
                unit(BL, c, False, False, True)
            with pool.Fori(0, NCH) as c:
                unit(B - 1, c, False, False, True)
            with pool.Fori(NU - NT, NU) as e:
                out_rsqrt(e)
                out_affine(e)

        @block.scalar
        def _(act):
            act.preload_act_table(ACT.Exp)
            act.wait_ge(s_cred, 1)

            def gelu_inputs(k, J):
                for j in J:
                    act.wait_ge(s_hp, ONE + k + j + 1)
                    act.activation(ab[:, j, :], hp[:, j, :], ACT.Abs)
                    act.activation(ex[:, j, :], hp[:, j, :], ACT.Square, scale=RSQRT2)

            def gelu_exp(k, J):
                act.drain()
                for j in J:
                    act.activation(ex[:, j, :], ex[:, j, :], ACT.Exp, scale=-1.0).then_inc(s_ex, 1)

            def unit(b, c, first, p, e):
                n = b * NCH + c
                k = n + LEAD
                for s in range(SLOTS):
                    if p and s == 11:
                        gelu_inputs(k, [0])
                    if p and s == 12:
                        gelu_exp(k, [0])
                    act.wait_ge(s_sc, ONE + n * SLOTS + s + 1)
                    if s % 2 == 0:
                        act.wait_ge(s_pv, n * NT + s // 2 + 1)
                    act.activation(prob[:, s % PROBS, :, :], PS[0:T, 2 * (s % RING):2 * (s % RING) + 2, 0:QC],
                                   ACT.Exp, scale=SCALE).then_inc(s_pr, 1)

            with act.Fori(0, LEAD // PGRP) as i:
                gelu_inputs(i * PGRP, range(PGRP))
                gelu_exp(i * PGRP, range(PGRP))
            unit(0, 0, True, True, False)
            with act.Fori(1, NCH) as c:
                unit(0, c, False, True, False)
            with act.Fori(1, BL) as b:
                with act.Fori(0, NCH) as c:
                    unit(b, c, False, True, True)
            with act.Fori(0, CL) as c:
                unit(BL, c, False, True, True)
            with act.Fori(CL, NCH) as c:
                unit(BL, c, False, False, True)
            with act.Fori(0, NCH) as c:
                unit(B - 1, c, False, False, True)

        @block.vector
        def _(dve):
            dve.memset(On[:, :], 0.0).then_inc(s_zeros, 1)
            dve.memset(KA[96:KROWS, :, :, :], 1.0)
            dve.memset(xT[:, :, :], 1.0)
            dve.memset(Vst[:, :, :, :], 1.0)
            dve.memset(Den[:, :], 1.0).then_inc(s_fill, 1)
            dve.wait_ge(s_fill, 1)
            dve.wait_ge(s_cred, 1)
            dve.wait_ge(s_w, 16 * WLOADS)

            def tok_stats(k, J, bank):
                for j in J:
                    dve.wait_ge(s_tok, ONE + k + j + 1)
                    dve.bn_stats(stat[:, j, :], PS[0:T, bank + j, 0:D])
                dve.drain()
                for j in J:
                    dve.bn_aggr(mv[:, j, :], stat[:, j, :]).then_inc(s_var, 1)

            def tok_norm(k, J, bank):
                for j in J:
                    dve.wait_ge(s_rs, ONE + k + j + 1)
                    dve.tensor_scalar(hp[:, j, :], PS[0:T, bank + j, 0:D], mv[:, j, 0:1], rs[:, j, :],
                                      ALU.subtract, ALU.mult).then_inc(s_nrm, 1)

            def take_zT(k, J, bank):
                for j in J:
                    dve.wait_ge(s_zT, ONE + k + j + 1)
                    dve.tensor_copy(zT[:, j, :, :], PS[:, bank + j, 0:KC * T].rearrange("p (c t) -> p c t", c=KC))\
                       .then_inc(s_zTs, 1)

            def take_qk(k, J, bank):
                bias = b_qk[:, :].unsqueeze(2).broadcast_to([128, 2 * KC, T])
                for j in J:
                    dve.wait_ge(s_sq, ONE + k)
                    dve.wait_ge(s_qk, ONE + k + j + 1)
                    dve.tensor_tensor(fq[:, j, :, :], PS[:, bank + j, 0:2 * KC * T].rearrange("p (c t) -> p c t", t=T),
                                      bias, ALU.add).then_inc(s_f, 1)

            def split(w, k, J):
                if w == 0:
                    dve.wait_ge(s_pst, ONE + 48 * k)
                for j in J:
                    ins = dve.tensor_copy(parts[:, j, w, :, :], fq[:, j, :, :])
                    if w == 2:
                        ins.then_inc(s_parts, 1)

            def rest(w, k, J):
                for j in J:
                    if w == 0:
                        dve.wait_ge(s_sq, ONE + k + j + 1)
                    dve.tensor_tensor(fq[:, j, :, :], fq[:, j, :, :], parts[:, j, w, :, :], ALU.subtract)

            def take_v(k, J, bank):
                for j in J:
                    dve.wait_ge(s_v, ONE + k + j + 1)
                    kj = k + j
                    dve.tensor_tensor(Vb[:, (kj // NT) % VBUF, kj % NT, :], PS[0:T, bank + j, 0:D], b_v[:, :], ALU.add)\
                       .then_inc(s_vb, 1)

            def take_norms(k, J, bank):
                for j in J:
                    dve.wait_ge(s_ns, ONE + k + j + 1)
                    kj = k + j
                    dve.tensor_scalar(norms[:, (kj // NT) % VBUF, kj % NT, :], PS[0:T, bank + j, 0:2 * H],
                                      1.0, None, ALU.mult).then_inc(s_nm, 1)

            def gelu_step(i, k, J):
                for j in J:
                    t, q = tt[:, j, :], qq[:, j, :]
                    if i == 0:
                        dve.wait_ge(s_ex, ONE + k + j + 1)
                        dve.tensor_scalar(t, ab[:, j, :], ERF_P * RSQRT2, 1.0, ALU.mult, ALU.add)
                    elif i == 1:
                        dve.reciprocal(t, t)
                    elif i == 2:
                        dve.tensor_scalar(q, t, ERF_A[4], None, ALU.mult)
                    elif i <= 6:
                        dve.scalar_tensor_tensor(out=q, in0=q, scalar=ERF_A[6 - i], in1=t, op0=ALU.add, op1=ALU.mult)
                    elif i == 7:
                        dve.tensor_tensor(q, q, ex[:, j, :], ALU.mult)
                    elif i == 8:
                        dve.scalar_tensor_tensor(out=q, in0=ab[:, j, :], scalar=0.5, in1=q, op0=ALU.mult, op1=ALU.mult)
                    elif i == 9:
                        dve.wait_ge(s_hst, ONE + 16 * k)
                        dve.scalar_tensor_tensor(out=hh[:, j, :], in0=hp[:, j, :], scalar=0.0, in1=q,
                                                 op0=ALU.max, op1=ALU.subtract).then_inc(s_h, 1)
                    elif i == 10:
                        dve.bn_stats(stat2[:, j, :], hh[:, j, :])
                    elif i == 11:
                        dve.bn_aggr(mv2[:, j, :], stat2[:, j, :]).then_inc(s_var2, 1)
            GELU = 12

            def attn_norm(k, J):
                for j in J:
                    dve.wait_ge(s_rs2, ONE + k + j + 1)
                    dve.tensor_scalar(tt[:, j, :], hh[:, j, :], mv2[:, j, 0:1], rs2[:, j, :],
                                      ALU.subtract, ALU.mult).then_inc(s_z, 1)

            def stage_v(b, c, t0, t1):
                w = HG * HD
                src = Vb[:, b % VBUF, t0:t1, bass.ds((c // NC) * w, w)].rearrange("p t (h d) -> p t h d", d=HD)
                return dve.tensor_scalar(Vst[:, t0:t1, :, 0:HD], src, 1.0, None, ALU.mult)

            def take_sums(n):
                dve.wait_ge(s_dn, ONE + 64 * n)
                dve.wait_ge(s_pv, NT * (n + 1) + AHEAD)
                dve.tensor_copy(Osb[:, :], PS[:, PVB, 0:QC]).then_inc(s_ov, 1)

            def invert(n):
                dve.wait_ge(s_dn, ONE + 64 * (n + 1))
                dve.wait_ge(s_os, ONE + 64 * n)
                dve.reciprocal(On[:, :], Den[:, :])

            def normalise(n):
                dve.tensor_tensor(On[:, :], On[:, :], Osb[:, :], ALU.mult).then_inc(s_on, 1)

            def out_step(i, e):
                if i == 0:
                    dve.wait_ge(s_or, ONE + e)
                    dve.wait_ge(s_eo, ONE + e + 1)
                    dve.tensor_tensor(s1[:, :], PS[0:T, MISC, 0:D], hE[:, :], ALU.add).then_inc(s_s1, 1)
                elif i == 1:
                    dve.bn_stats(estat[:, :], s1[:, :])
                elif i == 2:
                    dve.bn_aggr(emv[:, :], estat[:, :]).then_inc(s_ev, 1)
                elif i == 3:
                    dve.wait_ge(s_ost, ONE + 16 * e)
                    dve.wait_ge(s_er, ONE + e + 1)
                    dve.tensor_scalar(y2[:, :], s1[:, :], emv[:, 0:1], ers[:, 1:2], ALU.subtract, ALU.mult)\
                       .then_inc(s_y2, 1)

            def range_of(b):
                dve.drain()
                dve.reduce_max(nmax[:, :], norms[:, b % VBUF, :, :].rearrange("p t h -> p h t"), AX.X)\
                   .then_inc(s_nmax, 1)
                dve.wait_ge(s_nall, ONE + b + 1)
                dve.tensor_tensor(nprod[:, 0:H], nall[0:1, 0:H], nall[0:1, H:2 * H], ALU.mult)
                dve.drain()
                dve.reduce_max(nprod[:, H:H + 1], nprod[:, 0:H], AX.X)
                dve.drain()
                dve.tensor_scalar(nprod[:, 0:1], nprod[:, H:H + 1], (BOUND / SCALE) ** 2, None, ALU.is_le)
                dve.drain()
                dve.tensor_scalar(flags[0:1, bass.ds(b, 1)], nprod[:, 0:1], 0.0, None, ALU.is_equal)\
                   .then_inc(s_flag, 1)

            def seam(b):
                dve.drain()
                flag = dve.value_load(flags[0:1, bass.ds(b, 1)], min_val=0, max_val=1)
                with dve.If(flag != 0):
                    with dve.Fori(0, NG) as g:
                        with dve.Fori(0, HG * NT // 2) as i:
                            for s in range(2):
                                dve.wait_ge(s_ms, ONE + (b * NG + g) * HG * NT + 2 * i + s + 1)
                                dve.reduce_max(mx[:, bass.ds(2 * i + s, 1)], PS[0:T, 3 * s:3 * s + 3, 0:QC], AX.XY)\
                                   .then_inc(s_mx, 1)
                        dve.wait_ge(s_mt, ONE + b * NG + g + 1)
                        dve.tensor_scalar(mf[:, :], PS[0:HG * NT, MISC, 0:T], -1.0, None, ALU.mult)\
                           .then_inc(s_mtT, 1)
                        dve.drain()
                        dve.wait_ge(s_cst, ONE + 16 * (b * NG + g))
                        for w in range(3):
                            ins = dve.tensor_copy(mparts[:, w, :], mf[:, :])
                            if w == 2:
                                ins.then_inc(s_mc, 1)
                            dve.drain()
                            if w < 2:
                                dve.tensor_tensor(mf[:, :], mf[:, :], mparts[:, w, :], ALU.subtract)
                                dve.drain()
                with dve.Else():
                    dve.sem_inc(s_mx, NG * HG * NT)
                    dve.sem_inc(s_mtT, NG)
                    dve.sem_inc(s_mc, NG)

            def unit(b, c, first, p, e):
                n = b * NCH + c
                k = n + LEAD
                J, second = [0], p and not first
                if not first:
                    dve.wait_ge(s_pv, NT * n - 3 + AHEAD)
                stage_v(b, c, 0, NT - 3)
                if second:
                    take_zT(k - 1, J, MISC)
                if not first:
                    take_sums(n - 1)
                stage_v(b, c, NT - 3, NT).then_inc(s_vst, 1)
                if p:
                    tok_stats(k, J, MISC)
                    tok_norm(k, J, MISC)
                if not first:
                    invert(n - 1)
                if second:
                    take_qk(k - 1, J, MISC)
                dve.drain()
                if not first:
                    normalise(n - 1)
                if second:
                    split(0, k - 1, J)
                    dve.drain()
                    rest(0, k - 1, J)
                    dve.drain()
                    split(1, k - 1, J)
                    dve.drain()
                    take_v(k - 1, J, MISC)
                    rest(1, k - 1, J)
                    dve.drain()
                    split(2, k - 1, J)
                    take_norms(k - 1, J, MISC)
                for i in range(GELU):
                    if p:
                        gelu_step(i, k, J)
                    if e and 6 <= i < 9:
                        out_step(i - 6, n - NT)
                    if p or 6 <= i < 9:
                        dve.drain()
                if p:
                    attn_norm(k, J)
                if e:
                    out_step(3, n - NT)
                dve.drain()

            with dve.Fori(0, LEAD // PGRP) as i:
                k, J = i * PGRP, range(PGRP)
                tok_stats(k, J, 0)
                tok_norm(k, J, 0)
                for step in range(GELU):
                    gelu_step(step, k, J)
                    dve.drain()
                attn_norm(k, J)
                take_zT(k, J, 0)
                take_qk(k, J, 0)
                dve.drain()
                for w in range(3):
                    split(w, k, J)
                    dve.drain()
                    if w < 2:
                        rest(w, k, J)
                        dve.drain()
                take_v(k, J, 0)
                take_norms(k, J, 0)
                dve.drain()
            range_of(0)
            dve.wait_ge(s_zero, 16 * ZLOADS)
            seam(0)
            unit(0, 0, True, True, False)
            with dve.Fori(1, RC) as c:
                unit(0, c, False, True, False)
            range_of(1)
            with dve.Fori(RC, NCH) as c:
                unit(0, c, False, True, False)
            with dve.Fori(1, BL) as b:
                seam(b)
                with dve.Fori(0, RC) as c:
                    unit(b, c, False, True, True)
                range_of(b + 1)
                with dve.Fori(RC, NCH) as c:
                    unit(b, c, False, True, True)
            seam(BL)
            with dve.Fori(0, CL) as c:
                unit(BL, c, False, True, True)
            k = B * NT - 1
            take_zT(k, [0], MISC)
            take_qk(k, [0], MISC)
            dve.drain()
            for w in range(3):
                split(w, k, [0])
                dve.drain()
                if w < 2:
                    rest(w, k, [0])
                    dve.drain()
            take_v(k, [0], MISC)
            take_norms(k, [0], MISC)
            dve.drain()
            range_of(B - 1)
            with dve.Fori(CL, NCH) as c:
                unit(BL, c, False, False, True)
            seam(B - 1)
            with dve.Fori(0, NCH) as c:
                unit(B - 1, c, False, False, True)
            take_sums(NU - 1)
            invert(NU - 1)
            dve.drain()
            normalise(NU - 1)
            with dve.Fori(NU - NT, NU) as e:
                for i in range(4):
                    out_step(i, e)
                    dve.drain()

        @block.tensor
        def _(pe):
            pe.wait_ge(s_w, 16 * WLOADS)
            pe.wait_ge(s_id, 1)
            pe.wait_ge(s_cred, 1)
            pe.wait_ge(s_fill, 1)

            def tokenize(k, J, bank):
                pe.wait_ge(s_x, ONE + 16 * (k + len(J)))
                for j in J:
                    pe.matmul(PS[0:T, bank + j, 0:D], xT[:, j, :], w_tok[:, :], start=True, stop=True)\
                      .then_inc(s_tok, 1)

            def turn(k, J, bank):
                for j in J:
                    pe.wait_ge(s_z, ONE + k + j + 1)
                    for c in range(KC):
                        last = pe.transpose(PS[:, bank + j, c * T:(c + 1) * T], tt[:, j, c * 128:(c + 1) * 128],
                                            ident[0:T, 0:T])
                    last.then_inc(s_zT, 1)

            def project(k, J, bank, which):
                for j in J:
                    pe.wait_ge(s_zTs, ONE + k + j + 1)
                    for w in which:
                        for m in range(KC):
                            o = (w * KC + m) * T
                            for c in range(KC):
                                last = pe.matmul(PS[:, bank + j, o:o + T], w_qk[:, c, w, m * 128:(m + 1) * 128],
                                                 zT[:, j, c, :], start=(c == 0), stop=(c == KC - 1))
                    if 1 in which:
                        last.then_inc(s_qk, 1)

            def values(k, J, bank):
                for j in J:
                    pe.wait_ge(s_f, ONE + k + j + 1)
                    for c in range(KC):
                        last = pe.matmul(PS[0:T, bank + j, 0:D], zT[:, j, c, :], w_v[:, c, :],
                                         start=(c == 0), stop=(c == KC - 1))
                    last.then_inc(s_v, 1)

            def norm_sums(k, J, bank):
                for j in J:
                    pe.wait_ge(s_sq, ONE + k + j + 1)
                    pe.wait_ge(s_vb, ONE + k + j + 1)
                    for m in range(2 * KC):
                        w = 128 // HD
                        last = pe.matmul(PS[0:T, bank + j, m * w:(m + 1) * w], sq[:, j, m, :], head_sel[:, :],
                                         start=True, stop=True)
                    last.then_inc(s_ns, 1)

            def output(e):
                pe.wait_ge(s_el, ONE + 32 * (e + 1))
                for c in range(KC):
                    last = pe.matmul(PS[0:T, MISC, 0:D], oT[:, c, :], w_o[:, c, :], start=(c == 0), stop=(c == KC - 1))
                last.then_inc(s_eo, 1)

            def scores(n, c, s):
                g, q = c // NC, c % NC
                t, pair = s // 2, s % 2
                pe.wait_ge(s_pr, n * SLOTS + s + 1)
                for i in range(2):
                    hd = 2 * pair + i
                    last = pe.matmul(PS[0:T, 2 * (s % RING) + i, 0:QC], KA[:, g % 2, hd, t * T:(t + 1) * T],
                                     QA[:, g % 2, hd, bass.ds(q * QC, QC)], start=True, stop=True)
                last.then_inc(s_sc, 1)

            def attend(n, t):
                if t == 0:
                    pe.wait_ge(s_vst, ONE + n + 1)
                    pe.wait_ge(s_ov, ONE + n)
                pe.wait_ge(s_pr, RING + n * SLOTS + 2 * t + 2)
                for hd in range(HG):
                    lo = 2 * HD * hd
                    last = pe.matmul(PS[lo:lo + 2 * HD, PVB, 0:QC], Vst[:, t, hd, :],
                                     prob[:, (2 * t + hd // 2) % PROBS, hd % 2, :],
                                     start=(t == 0), stop=(t == NT - 1))
                last.then_inc(s_pv, 1)

            def seam(b):
                wait(pe, s_flag, ONE + b + 1)
                flag = pe.value_load(flags[0:1, bass.ds(b, 1)], min_val=0, max_val=1)
                with pe.If(flag != 0):
                    wait(pe, s_pr, RING + b * NCH * SLOTS)
                    with pe.Fori(0, NG) as g:
                        wait(pe, s_ldm, ONE + 16 * 2 * TERMS * (b * NG + g + 1))
                        with pe.Fori(0, HG * NT // 2) as i:
                            for s in range(2):
                                pe.wait_ge(s_mx, (b * NG + g) * HG * NT + 2 * i + s + 1)
                                hd = (2 * i) // NT
                                qa = QA[0:MROW, 1, :, :].rearrange("k h q -> k (h q)")
                                for c in range(NC):
                                    last = pe.matmul(PS[0:T, 3 * s + c, 0:QC],
                                                     qa[:, bass.ds(hd * S + ((2 * i) % NT + s) * T, T)],
                                                     KA[0:MROW, 1, hd, c * QC:(c + 1) * QC], start=True, stop=True)
                                last.then_inc(s_ms, 1)
                        wait(pe, s_mx, 2 + (b * NG + g + 1) * HG * NT)
                        wait(pe, s_s1, ONE + 0)
                        pe.transpose(PS[0:HG * NT, MISC, 0:T], mx[:, :], ident[0:T, 0:T]).then_inc(s_mt, 1)
                        wait(pe, s_mtT, ONE + b * NG + g + 1)
                with pe.Else():
                    pe.sem_inc(s_ms, NG * HG * NT)
                    pe.sem_inc(s_mt, NG)
                wait(pe, s_rl, ONE + 16 * (b + 1))

            def unit(b, c, first, p, e):
                n = b * NCH + c
                k = n + LEAD
                J, second = [0], p and not first
                wait(pe, s_lda, ONE + 16 * GLOADS * (b * NG + c // NC + 1))
                for s in range(SLOTS):
                    scores(n, c, s)
                    if s % 2 == 0:
                        if s >= 4:
                            attend(n, (s - 4) // 2)
                        elif not first:
                            attend(n - 1, NT - 2 + s // 2)
                    if s == 1 and p:
                        pe.wait_ge(s_nm, ONE + k - 1)
                        if e:
                            pe.wait_ge(s_s1, ONE + n - NT)
                    if s == 1 and second:
                        turn(k - 1, J, MISC)
                    if s == 3 and p:
                        if second:
                            pe.wait_ge(s_zTs, ONE + k)
                        tokenize(k, J, MISC)
                    if s == 6 and second:
                        pe.wait_ge(s_nrm, ONE + k + 1)
                        project(k - 1, J, MISC, [0])
                    if s == 7 and second:
                        project(k - 1, J, MISC, [1])
                    if s == 12 and second:
                        values(k - 1, J, MISC)
                    if s == 15 and second:
                        norm_sums(k - 1, J, MISC)
                    if s == 18 and e:
                        if p:
                            pe.wait_ge(s_nm, ONE + k)
                        else:
                            pe.wait_ge(s_s1, ONE + n - NT)
                        output(n - NT)

            with pe.Fori(0, LEAD // PGRP) as i:
                k, J = i * PGRP, range(PGRP)
                pe.wait_ge(s_nm, ONE + k)
                tokenize(k, J, 0)
                turn(k, J, 0)
                project(k, J, 0, [0, 1])
                values(k, J, 0)
                norm_sums(k, J, 0)
            pe.wait_ge(s_nm, ONE + LEAD)
            seam(0)
            unit(0, 0, True, True, False)
            with pe.Fori(1, NCH) as c:
                unit(0, c, False, True, False)
            with pe.Fori(1, BL) as b:
                seam(b)
                with pe.Fori(0, NCH) as c:
                    unit(b, c, False, True, True)
            seam(BL)
            with pe.Fori(0, CL) as c:
                unit(BL, c, False, True, True)
            k = B * NT - 1
            pe.wait_ge(s_s1, ONE + NU - LEAD - NT)
            turn(k, [0], MISC)
            project(k, [0], MISC, [0, 1])
            values(k, [0], MISC)
            norm_sums(k, [0], MISC)
            pe.wait_ge(s_nm, ONE + k + 1)
            with pe.Fori(CL, NCH) as c:
                unit(BL, c, False, False, True)
            seam(B - 1)
            with pe.Fori(0, NCH) as c:
                unit(B - 1, c, False, False, True)
            attend(NU - 1, NT - 2)
            attend(NU - 1, NT - 1)
            with pe.Fori(NU - NT, NU) as e:
                pe.wait_ge(s_s1, ONE + e)
                output(e)


_OUT = ((8, 1500, 256), 'float32')


def kernel(**inputs):
    import numpy as _np
    import concourse.bacc as _bacc
    from concourse import mybir as _mybir
    from concourse.bass_utils import run_bass_kernel_spmd as _run

    given = {
        "x": _np.asarray(inputs["x"]).reshape(8, 125, 12, -1).transpose(0, 2, 3, 1),
        "tok_wT": _np.asarray(inputs["L0_tok_W"]).T, "tok_b": inputs["L0_tok_b"],
        "tok_g": inputs["L0_tok_ln_gamma"], "tok_be": inputs["L0_tok_ln_beta"],
        "wqT": _np.asarray(inputs["L0_attn_Wq"]).T, "bq": inputs["L0_attn_bq"],
        "wkT": _np.asarray(inputs["L0_attn_Wk"]).T, "bk": inputs["L0_attn_bk"],
        "wvT": _np.asarray(inputs["L0_attn_Wv"]).T, "bv": inputs["L0_attn_bv"],
        "woT": _np.asarray(inputs["L0_attn_Wo"]).T, "bo": inputs["L0_attn_bo"],
        "ln_g": inputs["L0_ffn_ln_g"], "ln_b": inputs["L0_ffn_ln_b"],
    }
    nc = _bacc.Bacc("TRN2", target_bir_lowering=False, num_devices=1)
    arrays, args = {}, []
    for name, value in given.items():
        a = _np.ascontiguousarray(value)
        arrays[f"in_{name}"] = a
        args.append(nc.dram_tensor(f"in_{name}", a.shape, _mybir.dt.from_np(a.dtype), kind="ExternalInput").ap())
    args.append(nc.dram_tensor("out_0", _OUT[0], _mybir.dt.from_np(_np.dtype(_OUT[1])), kind="ExternalOutput").ap())
    audio_tower(nc, *args)
    r = _run(nc, [arrays], core_ids=[0])
    return r.results[0]["out_0"]
```
